# Optimizing a Trainium2 kernel written in Bass

```python
import numpy as np
import jax
import jax.numpy as jnp

def _softmax(x, axis=-1):
    return jax.nn.softmax(x, axis=axis)

def _gelu(x):
    return jax.nn.gelu(x, approximate=True)

def _silu(x):
    return jax.nn.silu(x)

def _sigmoid(x):
    return jax.nn.sigmoid(x)

def _layernorm(x, axis=-1, eps=1e-05):
    m = jnp.mean(x, axis=axis, keepdims=True)
    v = jnp.var(x, axis=axis, keepdims=True)
    return (x - m) / jnp.sqrt(v + eps)

def _scatter_add(tgt, idx, src, axis=0):
    return tgt.at[idx].add(src)

def _segment_sum(src, seg, n):
    return jax.ops.segment_sum(src, seg, n)
kernel_name = 'mk_dlrm_tower_d1_rec_r8_6dd591'

def setup_inputs(seed: int=0):
    np.random.seed(seed)
    _w = jnp.asarray

    def _rec_inputs():
        import jax
        import jax.numpy as jnp
        _tk = jax.random.key(seed)
        dense_ctx = jax.random.normal(jax.random.fold_in(_tk, 190), (2048, 16), jnp.float32)
        ids = jnp.stack([jax.random.randint(jax.random.fold_in(_tk, 200 + f), (2048,), 0, v, jnp.int32) for f, v in enumerate([1000, 1000, 1250, 125000, 1250, 1000, 1250, 1000, 12500, 1000, 1000, 1250, 12500, 1250, 1000, 12500, 125000, 125000, 12500, 12500, 125000, 125000, 1000, 12500, 12500, 125000, 125000, 12500, 125000, 1250, 12500, 12500, 1000, 1000, 125000, 12500, 125000, 1250, 125000])], axis=1)
        tbl_0 = 0.05 * jax.random.normal(jax.random.fold_in(_tk, 500 + 0), (1000, 16), jnp.float32)
        tbl_1 = 0.05 * jax.random.normal(jax.random.fold_in(_tk, 500 + 1), (1000, 16), jnp.float32)
        tbl_2 = 0.05 * jax.random.normal(jax.random.fold_in(_tk, 500 + 2), (1250, 16), jnp.float32)
        tbl_3 = 0.05 * jax.random.normal(jax.random.fold_in(_tk, 500 + 3), (125000, 16), jnp.float32)
        tbl_4 = 0.05 * jax.random.normal(jax.random.fold_in(_tk, 500 + 4), (1250, 16), jnp.float32)
        tbl_5 = 0.05 * jax.random.normal(jax.random.fold_in(_tk, 500 + 5), (1000, 16), jnp.float32)
        tbl_6 = 0.05 * jax.random.normal(jax.random.fold_in(_tk, 500 + 6), (1250, 16), jnp.float32)
        tbl_7 = 0.05 * jax.random.normal(jax.random.fold_in(_tk, 500 + 7), (1000, 16), jnp.float32)
        tbl_8 = 0.05 * jax.random.normal(jax.random.fold_in(_tk, 500 + 8), (12500, 16), jnp.float32)
        tbl_9 = 0.05 * jax.random.normal(jax.random.fold_in(_tk, 500 + 9), (1000, 16), jnp.float32)
        tbl_10 = 0.05 * jax.random.normal(jax.random.fold_in(_tk, 500 + 10), (1000, 16), jnp.float32)
        tbl_11 = 0.05 * jax.random.normal(jax.random.fold_in(_tk, 500 + 11), (1250, 16), jnp.float32)
        tbl_12 = 0.05 * jax.random.normal(jax.random.fold_in(_tk, 500 + 12), (12500, 16), jnp.float32)
        tbl_13 = 0.05 * jax.random.normal(jax.random.fold_in(_tk, 500 + 13), (1250, 16), jnp.float32)
        tbl_14 = 0.05 * jax.random.normal(jax.random.fold_in(_tk, 500 + 14), (1000, 16), jnp.float32)
        tbl_15 = 0.05 * jax.random.normal(jax.random.fold_in(_tk, 500 + 15), (12500, 16), jnp.float32)
        tbl_16 = 0.05 * jax.random.normal(jax.random.fold_in(_tk, 500 + 16), (125000, 16), jnp.float32)
        tbl_17 = 0.05 * jax.random.normal(jax.random.fold_in(_tk, 500 + 17), (125000, 16), jnp.float32)
        tbl_18 = 0.05 * jax.random.normal(jax.random.fold_in(_tk, 500 + 18), (12500, 16), jnp.float32)
        tbl_19 = 0.05 * jax.random.normal(jax.random.fold_in(_tk, 500 + 19), (12500, 16), jnp.float32)
        tbl_20 = 0.05 * jax.random.normal(jax.random.fold_in(_tk, 500 + 20), (125000, 16), jnp.float32)
        tbl_21 = 0.05 * jax.random.normal(jax.random.fold_in(_tk, 500 + 21), (125000, 16), jnp.float32)
        tbl_22 = 0.05 * jax.random.normal(jax.random.fold_in(_tk, 500 + 22), (1000, 16), jnp.float32)
        tbl_23 = 0.05 * jax.random.normal(jax.random.fold_in(_tk, 500 + 23), (12500, 16), jnp.float32)
        tbl_24 = 0.05 * jax.random.normal(jax.random.fold_in(_tk, 500 + 24), (12500, 16), jnp.float32)
        tbl_25 = 0.05 * jax.random.normal(jax.random.fold_in(_tk, 500 + 25), (125000, 16), jnp.float32)
        tbl_26 = 0.05 * jax.random.normal(jax.random.fold_in(_tk, 500 + 26), (125000, 16), jnp.float32)
        tbl_27 = 0.05 * jax.random.normal(jax.random.fold_in(_tk, 500 + 27), (12500, 16), jnp.float32)
        tbl_28 = 0.05 * jax.random.normal(jax.random.fold_in(_tk, 500 + 28), (125000, 16), jnp.float32)
        tbl_29 = 0.05 * jax.random.normal(jax.random.fold_in(_tk, 500 + 29), (1250, 16), jnp.float32)
        tbl_30 = 0.05 * jax.random.normal(jax.random.fold_in(_tk, 500 + 30), (12500, 16), jnp.float32)
        tbl_31 = 0.05 * jax.random.normal(jax.random.fold_in(_tk, 500 + 31), (12500, 16), jnp.float32)
        tbl_32 = 0.05 * jax.random.normal(jax.random.fold_in(_tk, 500 + 32), (1000, 16), jnp.float32)
        tbl_33 = 0.05 * jax.random.normal(jax.random.fold_in(_tk, 500 + 33), (1000, 16), jnp.float32)
        tbl_34 = 0.05 * jax.random.normal(jax.random.fold_in(_tk, 500 + 34), (125000, 16), jnp.float32)
        tbl_35 = 0.05 * jax.random.normal(jax.random.fold_in(_tk, 500 + 35), (12500, 16), jnp.float32)
        tbl_36 = 0.05 * jax.random.normal(jax.random.fold_in(_tk, 500 + 36), (125000, 16), jnp.float32)
        tbl_37 = 0.05 * jax.random.normal(jax.random.fold_in(_tk, 500 + 37), (1250, 16), jnp.float32)
        tbl_38 = 0.05 * jax.random.normal(jax.random.fold_in(_tk, 500 + 38), (125000, 16), jnp.float32)
        _rk = jax.random.fold_in(_tk, 7)
        W_top1 = 0.0693375 * jax.random.normal(jax.random.fold_in(_tk, 801), (208, 512), jnp.float32)
        W_top2 = 0.0441942 * jax.random.normal(jax.random.fold_in(_tk, 802), (512, 256), jnp.float32)
        W_top3 = 0.0625 * jax.random.normal(jax.random.fold_in(_tk, 803), (256, 1), jnp.float32)
        b_top1 = jnp.zeros((512,), jnp.float32)
        b_top2 = jnp.zeros((256,), jnp.float32)
        return (dense_ctx, ids, tbl_0, tbl_1, tbl_2, tbl_3, tbl_4, tbl_5, tbl_6, tbl_7, tbl_8, tbl_9, tbl_10, tbl_11, tbl_12, tbl_13, tbl_14, tbl_15, tbl_16, tbl_17, tbl_18, tbl_19, tbl_20, tbl_21, tbl_22, tbl_23, tbl_24, tbl_25, tbl_26, tbl_27, tbl_28, tbl_29, tbl_30, tbl_31, tbl_32, tbl_33, tbl_34, tbl_35, tbl_36, tbl_37, tbl_38, W_top1, b_top1, W_top2, b_top2, W_top3)
    dense_ctx, ids, tbl_0, tbl_1, tbl_2, tbl_3, tbl_4, tbl_5, tbl_6, tbl_7, tbl_8, tbl_9, tbl_10, tbl_11, tbl_12, tbl_13, tbl_14, tbl_15, tbl_16, tbl_17, tbl_18, tbl_19, tbl_20, tbl_21, tbl_22, tbl_23, tbl_24, tbl_25, tbl_26, tbl_27, tbl_28, tbl_29, tbl_30, tbl_31, tbl_32, tbl_33, tbl_34, tbl_35, tbl_36, tbl_37, tbl_38, W_top1, b_top1, W_top2, b_top2, W_top3 = _rec_inputs()

    def _L0_rec_setup():
        import jax, jax.numpy as jnp
        import numpy as np
        key = jax.random.key(seed)
        k1, k2, k3 = jax.random.split(key, 3)
        B, F0, D = (1024, 39, 16)
        L = 128
        hash_x = jax.random.normal(k1, (B, F0, D), dtype=jnp.float32)
        W0 = jax.random.normal(k2, (F0 * F0, L), dtype=jnp.float32) * 0.05
        W1 = jax.random.normal(k3, (F0 * (L // 2), L), dtype=jnp.float32) * 0.05
        return {'hash_x': hash_x, 'W0': W0, 'W1': W1}
    _L0_rec_all = _L0_rec_setup()
    _L0_rec_in = {k: v for k, v in _L0_rec_all.items() if k in ('W0', 'W1')}
    del _L0_rec_all
    return {'dense_ctx': dense_ctx, 'ids': ids, 'tbl_0': tbl_0, 'tbl_1': tbl_1, 'tbl_2': tbl_2, 'tbl_3': tbl_3, 'tbl_4': tbl_4, 'tbl_5': tbl_5, 'tbl_6': tbl_6, 'tbl_7': tbl_7, 'tbl_8': tbl_8, 'tbl_9': tbl_9, 'tbl_10': tbl_10, 'tbl_11': tbl_11, 'tbl_12': tbl_12, 'tbl_13': tbl_13, 'tbl_14': tbl_14, 'tbl_15': tbl_15, 'tbl_16': tbl_16, 'tbl_17': tbl_17, 'tbl_18': tbl_18, 'tbl_19': tbl_19, 'tbl_20': tbl_20, 'tbl_21': tbl_21, 'tbl_22': tbl_22, 'tbl_23': tbl_23, 'tbl_24': tbl_24, 'tbl_25': tbl_25, 'tbl_26': tbl_26, 'tbl_27': tbl_27, 'tbl_28': tbl_28, 'tbl_29': tbl_29, 'tbl_30': tbl_30, 'tbl_31': tbl_31, 'tbl_32': tbl_32, 'tbl_33': tbl_33, 'tbl_34': tbl_34, 'tbl_35': tbl_35, 'tbl_36': tbl_36, 'tbl_37': tbl_37, 'tbl_38': tbl_38, 'W_top1': W_top1, 'b_top1': b_top1, 'W_top2': W_top2, 'b_top2': b_top2, 'W_top3': W_top3, 'L0_rec_W0': _L0_rec_in['W0'], 'L0_rec_W1': _L0_rec_in['W1']}

def reference(dense_ctx, ids, tbl_0, tbl_1, tbl_2, tbl_3, tbl_4, tbl_5, tbl_6, tbl_7, tbl_8, tbl_9, tbl_10, tbl_11, tbl_12, tbl_13, tbl_14, tbl_15, tbl_16, tbl_17, tbl_18, tbl_19, tbl_20, tbl_21, tbl_22, tbl_23, tbl_24, tbl_25, tbl_26, tbl_27, tbl_28, tbl_29, tbl_30, tbl_31, tbl_32, tbl_33, tbl_34, tbl_35, tbl_36, tbl_37, tbl_38, W_top1, b_top1, W_top2, b_top2, W_top3, L0_rec_W0, L0_rec_W1):
    import jax
    import jax.numpy as jnp

    def _L0_rec_ref(hash_x, W0, W1):
        import jax, jax.numpy as jnp
        import numpy as np
        x0 = hash_x
        B, F0, D = x0.shape
        L = W0.shape[1]
        z0 = jnp.einsum('bid,bjd->bdij', x0, x0).reshape(B, D, F0 * F0)
        cur0 = jax.nn.relu(jnp.einsum('bdk,kl->bld', z0, W0))
        next_h, direct0 = jnp.split(cur0, 2, axis=1)
        Fk = next_h.shape[1]
        z1 = jnp.einsum('bid,bjd->bdij', x0, next_h).reshape(B, D, F0 * Fk)
        cur1 = jax.nn.relu(jnp.einsum('bdk,kl->bld', z1, W1))
        result = jnp.concatenate([direct0, cur1], axis=1)
        return jnp.sum(result, axis=-1)
    e = jnp.stack([tbl_0[ids[:, 0]], tbl_1[ids[:, 1]], tbl_2[ids[:, 2]], tbl_3[ids[:, 3]], tbl_4[ids[:, 4]], tbl_5[ids[:, 5]], tbl_6[ids[:, 6]], tbl_7[ids[:, 7]], tbl_8[ids[:, 8]], tbl_9[ids[:, 9]], tbl_10[ids[:, 10]], tbl_11[ids[:, 11]], tbl_12[ids[:, 12]], tbl_13[ids[:, 13]], tbl_14[ids[:, 14]], tbl_15[ids[:, 15]], tbl_16[ids[:, 16]], tbl_17[ids[:, 17]], tbl_18[ids[:, 18]], tbl_19[ids[:, 19]], tbl_20[ids[:, 20]], tbl_21[ids[:, 21]], tbl_22[ids[:, 22]], tbl_23[ids[:, 23]], tbl_24[ids[:, 24]], tbl_25[ids[:, 25]], tbl_26[ids[:, 26]], tbl_27[ids[:, 27]], tbl_28[ids[:, 28]], tbl_29[ids[:, 29]], tbl_30[ids[:, 30]], tbl_31[ids[:, 31]], tbl_32[ids[:, 32]], tbl_33[ids[:, 33]], tbl_34[ids[:, 34]], tbl_35[ids[:, 35]], tbl_36[ids[:, 36]], tbl_37[ids[:, 37]], tbl_38[ids[:, 38]]], axis=1)
    z = _L0_rec_ref(e, L0_rec_W0, L0_rec_W1)
    z = z.reshape(z.shape[0], -1)
    h = jnp.concatenate([z, dense_ctx], axis=1)
    h = jnp.maximum(h @ W_top1 + b_top1, 0.0)
    h = jnp.maximum(h @ W_top2 + b_top2, 0.0)
    y = h @ W_top3
    return y

_drawn_inputs = setup_inputs


def setup_inputs(seed=0):
    import zlib

    import numpy as np

    out = dict(_drawn_inputs(seed))
    spreads = {'b_top1': (0.0, 0.8), 'b_top2': (0.0, 0.439)}
    factors = {'tbl_0': 8.0,
     'tbl_1': 8.0,
     'tbl_2': 8.0,
     'tbl_3': 8.0,
     'tbl_4': 8.0,
     'tbl_5': 8.0,
     'tbl_6': 8.0,
     'tbl_7': 8.0,
     'tbl_8': 8.0,
     'tbl_9': 8.0,
     'tbl_10': 8.0,
     'tbl_11': 8.0,
     'tbl_12': 8.0,
     'tbl_13': 8.0,
     'tbl_14': 8.0,
     'tbl_15': 8.0,
     'tbl_16': 8.0,
     'tbl_17': 8.0,
     'tbl_18': 8.0,
     'tbl_19': 8.0,
     'tbl_20': 8.0,
     'tbl_21': 8.0,
     'tbl_22': 8.0,
     'tbl_23': 8.0,
     'tbl_24': 8.0,
     'tbl_25': 8.0,
     'tbl_26': 8.0,
     'tbl_27': 8.0,
     'tbl_28': 8.0,
     'tbl_29': 8.0,
     'tbl_30': 8.0,
     'tbl_31': 8.0,
     'tbl_32': 8.0,
     'tbl_33': 8.0,
     'tbl_34': 8.0,
     'tbl_35': 8.0,
     'tbl_36': 8.0,
     'tbl_37': 8.0,
     'tbl_38': 8.0,
     'L0_rec_W1': 8.0}
    for name, (base, spread) in spreads.items():
        noise = np.random.default_rng([zlib.crc32(name.encode()), seed]).standard_normal(out[name].shape)
        drawn = base * np.exp(spread * noise) if base else spread * noise
        out[name] = jnp.asarray(drawn.astype(out[name].dtype))
    for name, factor in factors.items():
        out[name] = (out[name] * factor).astype(out[name].dtype)
    return out
```

```python
import concourse.bass as bass
from concourse import mybir
from contextlib import ExitStack

P = 128
B = 2048
F = 39
D = 16
L = 128
H = L // 2
TILES = B // P
COLS = D * P
BANK = 512

SH = 3
STEPS0 = 7
SHIFTS = F // 2 + 1
ROWS0 = SH * F
Q, V = 8, 5
G, U = 16, 4
STEPS1 = U * V
STEPS = STEPS0 + STEPS1
RING = F + SHIFTS
RING = 59
NZ = 3
NX = 3
NA = 2
M1, M2 = 512, 256
K1, K2 = M1 // P, M2 // P
CH = B // BANK
DENSE = 16

FP = mybir.dt.float32
U32 = mybir.dt.uint32
ALU = mybir.AluOpType
ACT = mybir.ActivationFunctionType


def step_rows(s):
    return F * min(SH, SHIFTS - SH * s)


def at0(j, s):
    return s if isinstance(j, int) and j == 0 else j * STEPS - STEPS1 + s


def at1(j, s):
    return TILES * STEPS - STEPS1 + s if isinstance(j, int) and j == TILES - 1 else j * STEPS + 2 * STEPS0 + s


def slot0(j, s):
    return (s if isinstance(j, int) and j == 0 else s - STEPS1) % NZ


def slot1(j, s):
    return (s - STEPS1 if isinstance(j, int) and j == TILES - 1 else s + 2 * STEPS0) % NZ


def tower(nc, dense_ctx, ids, tables, W_top1, b_top1, W_top2, b_top2, W_top3, W0, W1, y):
    ctx = ExitStack()
    with ctx:
        ctx.enter_context(nc.allow_non_contiguous_dma(reason="biases and the last weights, once"))

        def sb(name, shape, dt=FP):
            return ctx.enter_context(nc.sbuf_tensor(name, shape, dt))

        def sem(name):
            return ctx.enter_context(nc.semaphore(name))

        x_rows = nc.dram_tensor("x_rows", [TILES, RING, COLS], FP, kind="Internal").ap()
        h_rows = nc.dram_tensor("h_rows", [TILES, H, COLS], FP, kind="Internal").ap()

        ident = sb("ident", [P, P])
        ids_all = sb("ids_all", [P, TILES, F], U32)
        ids_now = sb("ids_now", [P, F], U32)
        dense_all = sb("dense_all", [P, TILES, DENSE])
        emb = sb("emb", [P, F * D])
        x_now = sb("x_now", [F, COLS])
        x_base = sb("x_base", [ROWS0, COLS])
        x_first = sb("x_first", [ROWS0, COLS])
        x_shift = [sb(f"x_shift{n}", [ROWS0, COLS]) for n in range(NX)]
        x_lay = [sb(f"x_lay{v}", [P, COLS]) for v in range(V)]
        h_lay = [sb(f"h_lay{n}", [P, COLS]) for n in range(NA)]
        z = [sb(f"z{n}", [P, COLS]) for n in range(NZ)]
        r0 = sb("r0", [P, COLS])
        r1 = sb("r1", [P, COLS])
        w0 = sb("w0", [ROWS0, STEPS0, L])
        w1 = sb("w1", [P, V, U, L])
        wt1c = sb("wt1c", [P, M1])
        wt1d = sb("wt1d", [P, M1])
        wt2 = sb("wt2", [P, K1, M2])
        wt3 = sb("wt3", [P, K2])
        b1 = sb("b1", [P, K1])
        b2 = sb("b2", [P, K2])
        feat_d = sb("feat_d", [P, B])
        feat_c = sb("feat_c", [P, B])
        y_row = sb("y_row", [1, B])
        w0t = r1[0:ROWS0, 0:STEPS0 * L].rearrange("p (s l) -> p s l", s=STEPS0)
        hid1 = [x_lay[n][:, :].rearrange("p (k c) -> p k c", k=K1) for n in range(2)]
        hid2 = [x_lay[2 + n][:, 0:K2 * BANK].rearrange("p (k c) -> p k c", k=K2) for n in range(2)]

        psA = ctx.enter_context(nc.psum_tensor("psA", [P, COLS], FP))
        psB = ctx.enter_context(nc.psum_tensor("psB", [P, COLS], FP))

        ids_loaded = sem("ids_loaded")
        ids_set = sem("ids_set")
        dense_loaded = sem("dense_loaded")
        ident_zero = sem("ident_zero")
        ident_made = sem("ident_made")
        w0_zero = sem("w0_zero")
        w1_zero = sem("w1_zero")
        wt1_zero = sem("wt1_zero")
        feat_zero = sem("feat_zero")
        w0_loaded = sem("w0_loaded")
        w0_made = sem("w0_made")
        w1_loaded = sem("w1_loaded")
        top_loaded = sem("top_loaded")
        dense_turned = sem("dense_turned")
        dense_kept = sem("dense_kept")
        gathered = sem("gathered")
        x_turned = sem("x_turned")
        x_kept = sem("x_kept")
        x_stored = sem("x_stored")
        base_loaded = sem("base_loaded")
        first_loaded = sem("first_loaded")
        shift_loaded = [sem(f"shift_loaded{n}") for n in range(NX)]
        lay_loaded = [sem(f"lay_loaded{v}") for v in range(V)]
        hlay_loaded = [sem(f"hlay_loaded{n}") for n in range(NA)]
        z_made = sem("z_made")
        z_used = sem("z_used")
        mm0_done = sem("mm0_done")
        mm1_done = sem("mm1_done")
        relu0_done = sem("relu0_done")
        relu1_done = sem("relu1_done")
        h_stored = sem("h_stored")
        sum_step = sem("sum_step")
        sum0_done = sem("sum0_done")
        sum1_done = sem("sum1_done")
        top1_done = sem("top1_done")
        top1_kept = sem("top1_kept")
        top2_done = sem("top2_done")
        top2_kept = sem("top2_kept")
        top3_done = sem("top3_done")
        y_kept = sem("y_kept")
        y_stored = sem("y_stored")
        pool_passed = sem("pool_passed")
        pe_passed = sem("pe_passed")
        sp_passed = sem("sp_passed")

        block = ctx.enter_context(nc.Block())

        @block.sync
        def _(sp):
            def wait(done, value):
                sp.wait_ge(done, value)
                sp.sem_inc(sp_passed, 1)

            def load_shift(j, s, dst, loaded):
                for k in range(step_rows(s) // F):
                    a = SH * s + k
                    sp.dma_start(dst[k * F:(k + 1) * F, :], x_rows[j, a:a + F, :]).then_inc(loaded, 16)

            def load_base(j):
                if not (isinstance(j, int) and j == 0):
                    wait(z_made, at0(j - 1, STEPS0 - 1) + 1)
                for k in range(SH):
                    sp.dma_start(x_base[k * F:(k + 1) * F, :], x_rows[j, 0:F, :]).then_inc(base_loaded, 16)
                load_shift(j, 0, x_first, first_loaded)

            def load_early_shifts(j):
                for s in range(1, 1 + NX):
                    load_shift(j, s, x_shift[s - 1], shift_loaded[s - 1])

            def load_late_shifts(j):
                for s in range(1 + NX, STEPS0):
                    wait(z_made, at0(j, s - NX) + 1)
                    load_shift(j, s, x_shift[(s - 1) % NX], shift_loaded[(s - 1) % NX])

            def load_lay(j, v):
                src = x_rows[j, v:v + V * (Q - 1) + 1:V, :].unsqueeze(0).to_broadcast([G, Q, COLS])
                sp.dma_start(x_lay[v][:, :], src).then_inc(lay_loaded[v], 16)

            def load_hlay(j, u):
                src = h_rows[j, u:u + U * (G - 1) + 1:U, :].unsqueeze(1).to_broadcast([G, Q, COLS])
                sp.dma_start(h_lay[u % NA][:, :], src).then_inc(hlay_loaded[u % NA], 16)

            def store_x(j):
                wait(x_kept, j + 1)
                sp.dma_start(x_rows[j, 0:F, :], x_now[:, :]).then_inc(x_stored, 16)
                sp.dma_start(x_rows[j, F:RING, :], x_now[0:RING - F, :]).then_inc(x_stored, 16)
                wait(x_stored, 32 * j + 32)

            def store_h(j):
                wait(relu0_done, j + 1)
                sp.dma_start(h_rows[j, :, :], r0[0:H, :]).then_inc(h_stored, 16)

            def load_first_hlays(j):
                if not (isinstance(j, int) and j == 0):
                    wait(z_made, at1(j - 1, (U - 1) * V - 1) + 1)
                wait(h_stored, 16 * j + 16)
                load_hlay(j, 0)
                for v in range(V):
                    if not (isinstance(j, int) and j == 0):
                        wait(z_made, at1(j - 1, (U - 1) * V + v) + 1)
                    load_lay(j, v)
                load_hlay(j, 1)

            def load_hlay_after(j, u):
                wait(z_made, at1(j, (u - 1) * V - 1) + 1)
                load_hlay(j, u)

            def body(j, turn):
                load_late_shifts(j)
                store_h(j)
                load_hlay_after(j - 1, 2)
                if turn:
                    store_x(j + 1)
                    load_base(j + 1)
                    load_early_shifts(j + 1)
                load_hlay_after(j - 1, 3)
                load_first_hlays(j)

            sp.dma_start(ids_all[:, :, :], ids.bitcast(U32).rearrange("(t p) f -> p t f", p=P)).then_inc(ids_loaded, 16)
            sp.dma_start(dense_all[:, :, :], dense_ctx.rearrange("(t p) f -> p t f", p=P)).then_inc(dense_loaded, 16)

            sp.wait_ge(w0_zero, 1)
            for a in range(SHIFTS):
                s, k = divmod(a, SH)
                parts = [(0, F - a, F + 1, a, F * a)]
                if a:
                    parts.append((F - a, a, F + 1, (F + 1) * (F - a) + a - F, (F + 1) * (F - a) + F * (a - F)))
                for i0, n, step, row, row_t in parts:
                    p = k * F + i0
                    sp.dma_start(w0[p:p + n, s, :], W0[row:row + step * (n - 1) + 1:step, :]).then_inc(w0_loaded, 16)
                    if a:
                        sp.dma_start(w0t[p:p + n, s, :],
                                     W0[row_t:row_t + step * (n - 1) + 1:step, :]).then_inc(w0_loaded, 16)

            store_x(0)
            load_base(0)
            load_early_shifts(0)
            load_late_shifts(0)

            sp.wait_ge(w1_zero, 1)
            for i in range(F):
                q, v = divmod(i, V)
                sp.dma_start(w1[q:q + Q * (G - 1) + 1:Q, v, :, :],
                             W1[i * H:(i + 1) * H, :].rearrange("(g u) l -> g u l", u=U)).then_inc(w1_loaded, 16)
            store_x(1)
            load_base(1)
            load_early_shifts(1)
            store_h(0)
            load_first_hlays(0)

            sp.wait_ge(wt1_zero, 1)
            sp.dma_start(wt1d[H:P, :], W_top1[0:H, :]).then_inc(top_loaded, 16)
            sp.dma_start(wt1c[:, :], W_top1[H:H + L, :]).then_inc(top_loaded, 16)
            sp.dma_start(wt1d[0:DENSE, :], W_top1[H + L:H + L + DENSE, :]).then_inc(top_loaded, 16)
            sp.dma_start(wt2[:, :, :], W_top2.rearrange("(k p) n -> p k n", p=P)).then_inc(top_loaded, 16)
            sp.dma_start(wt3[:, :], W_top3.rearrange("(k p) o -> p (k o)", p=P)).then_inc(top_loaded, 16)
            sp.dma_start(b1[:, :], b_top1.rearrange("(k p) -> p k", p=P)).then_inc(top_loaded, 16)
            sp.dma_start(b2[:, :], b_top2.rearrange("(k p) -> p k", p=P)).then_inc(top_loaded, 16)

            with sp.Fori(1, TILES - 1) as j:
                body(j, True)
            body(TILES - 1, False)
            for u in range(2, U):
                load_hlay_after(TILES - 1, u)
            sp.wait_ge(y_kept, CH)
            sp.dma_start(y.rearrange("b o -> o b"), y_row[:, :]).then_inc(y_stored, 16)
            sp.wait_ge(y_stored, 16)

        @block.gpsimd
        def _(pool):
            def gather(j):
                if not (isinstance(j, int) and j == 0):
                    pool.wait_ge(x_turned, j)
                nc.gpsimd.tensor_copy(ids_now[:, :], ids_all[:, bass.ds(j, 1), :].rearrange("p t f -> p (t f)")).then_inc(ids_set, 1)
                pool.wait_ge(ids_set, j + 1)
                pool.sem_inc(pool_passed, 1)
                for f in range(F):
                    nc.gpsimd.indirect_dma_start(emb[:, f * D:(f + 1) * D], None, tables[f],
                                                 bass.IndirectOffsetOnAxis(ids_now[:, f:f + 1], 0)).then_inc(gathered, 16)

            nc.gpsimd.memset(w0[:, :, :], 0.0)
            nc.gpsimd.memset(w0t, 0.0).then_inc(w0_zero, 1)
            nc.gpsimd.memset(ident[:, :], 0.0).then_inc(ident_zero, 1)
            pool.wait_ge(ident_zero, 1)
            nc.gpsimd.affine_select(out=ident[:, :], in_=ident[:, :], compare_op=ALU.not_equal, fill=1.0, base=0,
                                    pattern=[[-1, P]], channel_multiplier=1).then_inc(ident_made, 1)
            pool.wait_ge(ids_loaded, 16)
            gather(0)
            nc.gpsimd.memset(w1[:, V - 1, :, :], 0.0).then_inc(w1_zero, 1)
            nc.gpsimd.memset(wt1d[:, :], 0.0).then_inc(wt1_zero, 1)
            nc.gpsimd.memset(feat_d[:, :], 0.0).then_inc(feat_zero, 1)
            with pool.Fori(1, TILES) as j:
                gather(j)

        @block.tensor
        def _(pe):
            def turn_x(j):
                pe.wait_ge(gathered, 16 * F * j + 16 * F)
                if not (isinstance(j, int) and j == 0):
                    pe.wait_ge(relu0_done, j)
                pe.sem_inc(pe_passed, 1)
                e = emb[:, :].rearrange("p (f d) -> p d f", d=D)
                for d in range(D):
                    last = nc.tensor.transpose(psA[0:F, d * P:(d + 1) * P], e[:, d, :], ident[:, :])
                last.then_inc(x_turned, 1)

            def product(ps, place, slot, k, w, first, last_step, done):
                pe.wait_ge(z_made, place + 1)
                for c in range(COLS // BANK):
                    mm = nc.tensor.matmul(ps[:, c * BANK:(c + 1) * BANK], w, z[slot][0:k, c * BANK:(c + 1) * BANK],
                                          start=first, stop=last_step)
                mm.then_inc(z_used, 1)

            def layer0(j):
                pe.wait_ge(x_kept, j + 1)
                for s in range(STEPS0):
                    product(psA, at0(j, s), slot0(j, s), step_rows(s), w0[0:step_rows(s), s, :],
                            s == 0, s == STEPS0 - 1, mm0_done)

            def layer1(j, steps):
                for s in steps:
                    u, v = divmod(s, V)
                    product(psB, at1(j, s), slot1(j, s), P, w1[:, v, u, :], s == 0, s == STEPS1 - 1, mm1_done)

            def body(j, turn):
                layer0(j)
                if not (isinstance(j, int) and j == 1):
                    pe.wait_ge(relu1_done, j - 1)
                layer1(j - 1, range(0, 4))
                if turn:
                    turn_x(j + 1)
                layer1(j - 1, range(4, STEPS1))

            pe.wait_ge(ident_made, 1)
            pe.wait_ge(dense_loaded, 16)
            for t in range(TILES):
                last = nc.tensor.transpose(psB[0:DENSE, t * P:(t + 1) * P], dense_all[:, t, :], ident[:, :])
            last.then_inc(dense_turned, 1)
            turn_x(0)
            pe.wait_ge(w0_made, 1)
            layer0(0)
            turn_x(1)
            pe.wait_ge(w1_loaded, 16 * F)
            pe.wait_ge(dense_kept, 1)
            body(1, True)
            with pe.Fori(2, TILES - 1) as j:
                body(j, True)
            body(TILES - 1, False)
            pe.wait_ge(relu1_done, TILES - 1)
            layer1(TILES - 1, range(STEPS1))

            def top1(c):
                cs = slice(c * BANK, (c + 1) * BANK)
                for m in range(K1):
                    if c:
                        pe.wait_ge(top1_kept, (c - 1) * K1 + m + 1)
                    nc.tensor.matmul(psA[:, m * BANK:(m + 1) * BANK], wt1c[:, m * P:(m + 1) * P], feat_c[:, cs],
                                     start=True, stop=False)
                    nc.tensor.matmul(psA[:, m * BANK:(m + 1) * BANK], wt1d[:, m * P:(m + 1) * P], feat_d[:, cs],
                                     start=False, stop=True).then_inc(top1_done, 1)

            pe.wait_ge(top_loaded, 16 * 7)
            pe.wait_ge(feat_zero, 1)
            pe.wait_ge(sum0_done, TILES)
            pe.wait_ge(sum1_done, TILES)
            top1(0)
            for c in range(CH):
                if c + 1 < CH:
                    top1(c + 1)
                for m in range(K2):
                    if c:
                        pe.wait_ge(top2_kept, (c - 1) * K2 + m + 1)
                    for k in range(K1):
                        pe.wait_ge(top1_kept, c * K1 + k + 1)
                        mm = nc.tensor.matmul(psB[:, m * BANK:(m + 1) * BANK], wt2[:, k, m * P:(m + 1) * P],
                                              hid1[c % 2][:, k, :], start=(k == 0), stop=(k == K1 - 1))
                    mm.then_inc(top2_done, 1)
                if c:
                    pe.wait_ge(y_kept, c)
                for k in range(K2):
                    pe.wait_ge(top2_kept, c * K2 + k + 1)
                    mm = nc.tensor.matmul(psB[0:1, K2 * BANK:(K2 + 1) * BANK], wt3[:, k:k + 1], hid2[c % 2][:, k, :],
                                          start=(k == 0), stop=(k == K2 - 1))
                mm.then_inc(top3_done, 1)

        @block.scalar
        def _(act):
            def keep_x(j):
                act.wait_ge(x_turned, j + 1)
                if not (isinstance(j, int) and j == 0):
                    act.wait_ge(x_stored, 32 * j)
                nc.scalar.activation(x_now[:, :], psA[0:F, :], ACT.Copy).then_inc(x_kept, 1)

            def relu0(j):
                act.wait_ge(z_used, at0(j, STEPS0 - 1) + 1)
                if not (isinstance(j, int) and j == 0):
                    act.wait_ge(h_stored, 16 * j)
                    act.wait_ge(sum0_done, j)
                nc.scalar.activation(r0[:, :], psA[:, :], ACT.Relu).then_inc(relu0_done, 1)

            def relu1(j):
                act.wait_ge(z_used, at1(j, STEPS1 - 1) + 1)
                if not (isinstance(j, int) and j == 0):
                    act.wait_ge(sum1_done, j)
                nc.scalar.activation(r1[:, :], psB[:, :], ACT.Relu).then_inc(relu1_done, 1)

            act.wait_ge(dense_turned, 1)
            act.wait_ge(feat_zero, 1)
            nc.scalar.activation(feat_d[0:DENSE, :], psB[0:DENSE, :], ACT.Copy).then_inc(dense_kept, 1)
            keep_x(0)
            relu0(0)
            keep_x(1)
            act.wait_ge(w0_made, 1)
            with act.Fori(1, TILES - 1) as j:
                relu0(j)
                keep_x(j + 1)
                relu1(j - 1)
            relu0(TILES - 1)
            relu1(TILES - 2)
            relu1(TILES - 1)

            act.wait_ge(top_loaded, 16 * 7)
            act.wait_ge(z_made, TILES * STEPS)

            def top1_keep(c):
                for m in range(K1):
                    act.wait_ge(top1_done, c * K1 + m + 1)
                    if c >= 2:
                        act.wait_ge(top2_done, (c - 1) * K2)
                    nc.scalar.activation(hid1[c % 2][:, m, :], psA[:, m * BANK:(m + 1) * BANK], ACT.Relu,
                                         bias=b1[:, m:m + 1]).then_inc(top1_kept, 1)

            top1_keep(0)
            for c in range(CH):
                if c + 1 < CH:
                    top1_keep(c + 1)
                for m in range(K2):
                    act.wait_ge(top2_done, c * K2 + m + 1)
                    if c >= 2:
                        act.wait_ge(top3_done, c - 1)
                    nc.scalar.activation(hid2[c % 2][:, m, :], psB[:, m * BANK:(m + 1) * BANK], ACT.Relu,
                                         bias=b2[:, m:m + 1]).then_inc(top2_kept, 1)
                act.wait_ge(top3_done, c + 1)
                nc.scalar.activation(y_row[:, c * BANK:(c + 1) * BANK], psB[0:1, K2 * BANK:(K2 + 1) * BANK],
                                     ACT.Copy).then_inc(y_kept, 1)

        @block.vector
        def _(dve):
            def make(place, slot, k, a, b):
                if not (isinstance(place, int) and place < NZ):
                    dve.wait_ge(z_used, place - NZ + 1)
                nc.vector.tensor_tensor(z[slot][0:k, :], a[0:k, :], b[0:k, :], ALU.mult).then_inc(z_made, 1)

            def layer0(j, steps):
                for s in steps:
                    if s == 0:
                        dve.wait_ge(base_loaded, 48 * j + 48)
                        dve.wait_ge(first_loaded, 48 * j + 48)
                        other = x_first
                    else:
                        n = (s - 1) % NX
                        first, both = 16 * (step_rows(n + 1) // F), 16 * ((step_rows(n + 1) + step_rows(n + 1 + NX)) // F)
                        dve.wait_ge(shift_loaded[n], both * j + (first if s <= NX else both))
                        other = x_shift[n]
                    make(at0(j, s), slot0(j, s), step_rows(s), x_base, other)

            def layer1(j, steps):
                for s in steps:
                    u, v = divmod(s, V)
                    if v == 0:
                        dve.wait_ge(hlay_loaded[u % NA], 32 * j + 16 * (u // NA) + 16)
                    if u == 0:
                        dve.wait_ge(lay_loaded[v], 16 * j + 16)
                    make(at1(j, s), slot1(j, s), P, h_lay[u % NA], x_lay[v])

            def sum_over_d(r, rows, n, out, done):
                width = COLS // 2
                for step in range(3):
                    nc.vector.tensor_tensor(r[rows, 0:width], r[rows, 0:width], r[rows, width:2 * width],
                                            ALU.add).then_inc(sum_step, 1)
                    dve.wait_ge(sum_step, 3 * n + step + 1)
                    width //= 2
                nc.vector.tensor_tensor(out, r[rows, 0:width], r[rows, width:2 * width], ALU.add).then_inc(done, 1)

            def sum0(j, n):
                dve.wait_ge(relu0_done, j + 1)
                sum_over_d(r0, slice(H, P), n, feat_d[H:P, bass.ds(j * P, P)], sum0_done)

            def sum1(j, n):
                dve.wait_ge(relu1_done, j + 1)
                sum_over_d(r1, slice(0, P), n, feat_c[:, bass.ds(j * P, P)], sum1_done)

            def body(j):
                layer0(j, range(0, 6))
                if not (isinstance(j, int) and j == 1):
                    sum1(j - 2, 2 * j - 2)
                layer0(j, range(6, STEPS0))
                layer1(j - 1, range(0, 6))
                sum0(j, 2 * j - 1)
                layer1(j - 1, range(6, STEPS1))

            dve.wait_ge(w0_loaded, 16 * (4 * SHIFTS - 3))
            nc.vector.tensor_tensor(w0[:, :, :], w0[:, :, :], w0t, ALU.add).then_inc(w0_made, 1)
            dve.wait_ge(feat_zero, 1)
            layer0(0, range(STEPS0))
            sum0(0, 0)
            body(1)
            with dve.Fori(2, TILES) as j:
                body(j)
            last = TILES - 1
            layer1(last, range(0, 6))
            sum1(last - 1, 2 * last)
            layer1(last, range(6, STEPS1))
            sum1(last, 2 * last + 1)


def kernel(**inputs):
    import numpy as np
    import concourse.bacc as bacc
    from concourse.bass_utils import run_bass_kernel_spmd

    nc = bacc.Bacc("TRN2", target_bir_lowering=False, num_devices=1)
    arrays = {}

    def given(name):
        a = np.ascontiguousarray(inputs[name])
        arrays[f"in_{name}"] = a
        return nc.dram_tensor(f"in_{name}", a.shape, mybir.dt.from_np(a.dtype), kind="ExternalInput").ap()

    y = nc.dram_tensor("out_y", (B, 1), FP, kind="ExternalOutput").ap()
    tower(nc, given("dense_ctx"), given("ids"), [given(f"tbl_{f}") for f in range(F)], given("W_top1"),
          given("b_top1"), given("W_top2"), given("b_top2"), given("W_top3"), given("L0_rec_W0"),
          given("L0_rec_W1"), y)
    r = run_bass_kernel_spmd(nc, [arrays], core_ids=[0])
    return r.results[0]["out_y"]
```

```python
import concourse.bass as bass
from concourse import mybir
from contextlib import ExitStack

P = 128
B = 2048
F = 39
D = 16
L = 128
H = L // 2
TILES = B // P
COLS = D * P
BANK = 512

SH = 3
STEPS0 = 7
SHIFTS = F // 2 + 1
ROWS0 = SH * F
Q, V = 8, 5
G, U = 16, 4
STEPS1 = U * V
STEPS = STEPS0 + STEPS1
RING = F + SHIFTS - 1
SPLIT0 = (1, 4)
SPLIT1 = (0, 3, 6, 9, 12, 15, 18)
SPLITS = len(SPLIT0) + len(SPLIT1)
WHOLE0 = tuple(s for s in range(STEPS0) if s not in SPLIT0)
WHOLE1 = tuple(s for s in range(STEPS1) if s not in SPLIT1)
NZ = 3
NX = 2
NA = 2
M1, M2 = 512, 256
K1, K2 = M1 // P, M2 // P
CH = B // BANK
DENSE = 16

FP = mybir.dt.float32
FR = mybir.dt.float32r
U32 = mybir.dt.uint32
ALU = mybir.AluOpType
ACT = mybir.ActivationFunctionType


def step_rows(s):
    return F * min(SH, SHIFTS - SH * s)


def at0(j, s):
    return s if isinstance(j, int) and j == 0 else j * STEPS - STEPS1 + s


def at1(j, s):
    return TILES * STEPS - STEPS1 + s if isinstance(j, int) and j == TILES - 1 else j * STEPS + 2 * STEPS0 + s


def slot0(j, s):
    return (WHOLE0.index(s) - (len(WHOLE0) if isinstance(j, int) and j == 0 else 0)) % NZ


def slot1(j, s):
    return (WHOLE1.index(s) + (0 if isinstance(j, int) and j == TILES - 1 else len(WHOLE0))) % NZ


def before0(j, s):
    n = WHOLE0.index(s) - NZ
    if n >= 0:
        return at0(j, WHOLE0[n])
    if isinstance(j, int) and j < 2:
        return at0(0, WHOLE0[n]) if j else None
    return at1(j - 2, WHOLE1[n])


def before1(j, s):
    n = WHOLE1.index(s) - NZ
    if n >= 0:
        return at1(j, WHOLE1[n])
    return at1(j - 1, WHOLE1[n]) if isinstance(j, int) and j == TILES - 1 else at0(j + 1, WHOLE0[n])


def split0(j, s):
    return SPLIT0.index(s) + (0 if isinstance(j, int) and j == 0 else j * SPLITS - len(SPLIT1))


def split1(j, s):
    last = isinstance(j, int) and j == TILES - 1
    return SPLIT1.index(s) + (TILES * SPLITS - len(SPLIT1) if last else j * SPLITS + 2 * len(SPLIT0))


def tower(nc, dense_ctx, ids, tables, W_top1, b_top1, W_top2, b_top2, W_top3, W0, W1, y):
    ctx = ExitStack()
    with ctx:
        ctx.enter_context(nc.allow_non_contiguous_dma(reason="biases and the last weights, once"))

        def sb(name, shape, dt=FP):
            return ctx.enter_context(nc.sbuf_tensor(name, shape, dt))

        def sem(name):
            return ctx.enter_context(nc.semaphore(name))

        x_rows = nc.dram_tensor("x_rows", [TILES, RING, COLS], FP, kind="Internal").ap()
        h_rows = nc.dram_tensor("h_rows", [TILES, H, COLS], FP, kind="Internal").ap()

        ident = sb("ident", [P, P])
        ids_all = sb("ids_all", [P, TILES, F], U32)
        ids_now = sb("ids_now", [P, F], U32)
        dense_all = sb("dense_all", [P, TILES, DENSE])
        emb = sb("emb", [P, F * D])
        x_base = sb("x_base", [ROWS0, COLS])
        x_first = sb("x_first", [ROWS0, COLS])
        x_shift = [sb(f"x_shift{n}", [ROWS0, COLS]) for n in range(NX)]
        x_lay = [sb(f"x_lay{v}", [P, COLS]) for v in range(V)]
        h_lay = [sb(f"h_lay{n}", [P, COLS]) for n in range(NA)]
        z = [sb(f"z{n}", [P, COLS]) for n in range(NZ)]
        z_split = sb("z_split", [P, COLS])
        z_hi = sb("z_hi", [P, COLS], FR)
        z_lo = sb("z_lo", [P, COLS], FR)
        r0 = sb("r0", [P, COLS])
        r1 = sb("r1", [P, COLS])
        w0 = sb("w0", [ROWS0, STEPS0, L])
        w0_hi = sb("w0_hi", [ROWS0, len(SPLIT0), L], FR)
        w0_lo = sb("w0_lo", [ROWS0, len(SPLIT0), L], FR)
        w1 = sb("w1", [P, V, U, L])
        w1_hi = sb("w1_hi", [P, len(SPLIT1), L], FR)
        w1_lo = sb("w1_lo", [P, len(SPLIT1), L], FR)
        wt1c = sb("wt1c", [P, M1])
        wt1d = sb("wt1d", [P, M1])
        wt2 = sb("wt2", [P, K1, M2])
        wt3 = sb("wt3", [P, K2])
        b1 = sb("b1", [P, K1])
        b2 = sb("b2", [P, K2])
        feat_d = sb("feat_d", [P, B])
        feat_c = sb("feat_c", [P, B])
        x_now = r1[0:F, :]
        w0t = h_lay[1][0:ROWS0, 0:STEPS0 * L].rearrange("p (s l) -> p s l", s=STEPS0)
        y_row = x_lay[4][0:1, :]
        hid1 = [x_lay[n][:, :].rearrange("p (k c) -> p k c", k=K1) for n in range(2)]
        hid2 = [x_lay[2 + n][:, 0:K2 * BANK].rearrange("p (k c) -> p k c", k=K2) for n in range(2)]

        psA = ctx.enter_context(nc.psum_tensor("psA", [P, COLS], FP))
        psB = ctx.enter_context(nc.psum_tensor("psB", [P, COLS], FP))

        ids_loaded = sem("ids_loaded")
        ids_set = sem("ids_set")
        dense_loaded = sem("dense_loaded")
        ident_zero = sem("ident_zero")
        ident_made = sem("ident_made")
        w0_zero = sem("w0_zero")
        w1_zero = sem("w1_zero")
        wt1_zero = sem("wt1_zero")
        feat_zero = sem("feat_zero")
        w0_loaded = sem("w0_loaded")
        w0_made = sem("w0_made")
        w1_loaded = sem("w1_loaded")
        w_hi_made = sem("w_hi_made")
        w_split = sem("w_split")
        top_loaded = sem("top_loaded")
        dense_turned = sem("dense_turned")
        dense_kept = sem("dense_kept")
        gathered = sem("gathered")
        x_turned = sem("x_turned")
        x_kept = sem("x_kept")
        x_stored = sem("x_stored")
        base_loaded = sem("base_loaded")
        first_loaded = sem("first_loaded")
        shift_loaded = [sem(f"shift_loaded{n}") for n in range(NX)]
        lay_loaded = [sem(f"lay_loaded{v}") for v in range(V)]
        hlay_loaded = [sem(f"hlay_loaded{n}") for n in range(NA)]
        z_made = sem("z_made")
        z_used = sem("z_used")
        z_hi_made = sem("z_hi_made")
        z_lo_made = sem("z_lo_made")
        relu0_done = sem("relu0_done")
        relu1_done = sem("relu1_done")
        h_stored = sem("h_stored")
        sum_step = sem("sum_step")
        sum0_done = sem("sum0_done")
        sum1_done = sem("sum1_done")
        top1_done = sem("top1_done")
        top1_kept = sem("top1_kept")
        top2_done = sem("top2_done")
        top2_kept = sem("top2_kept")
        top3_done = sem("top3_done")
        y_kept = sem("y_kept")
        y_stored = sem("y_stored")
        pool_passed = sem("pool_passed")
        pe_passed = sem("pe_passed")
        sp_passed = sem("sp_passed")

        block = ctx.enter_context(nc.Block())

        @block.sync
        def _(sp):
            def wait(done, value):
                sp.wait_ge(done, value)
                sp.sem_inc(sp_passed, 1)

            def load_shift(j, s, dst, loaded):
                for k in range(step_rows(s) // F):
                    a = SH * s + k
                    sp.dma_start(dst[k * F:(k + 1) * F, :], x_rows[j, a:a + F, :]).then_inc(loaded, 16)

            def load_base(j):
                if not (isinstance(j, int) and j == 0):
                    wait(z_made, at0(j - 1, STEPS0 - 1) + 1)
                for k in range(SH):
                    sp.dma_start(x_base[k * F:(k + 1) * F, :], x_rows[j, 0:F, :]).then_inc(base_loaded, 16)
                load_shift(j, 0, x_first, first_loaded)

            def load_early_shifts(j):
                for s in range(1, 1 + NX):
                    load_shift(j, s, x_shift[s - 1], shift_loaded[s - 1])

            def load_late_shifts(j):
                for s in range(1 + NX, STEPS0):
                    wait(z_made, at0(j, s - NX) + 1)
                    load_shift(j, s, x_shift[(s - 1) % NX], shift_loaded[(s - 1) % NX])

            def load_lay(j, v):
                src = x_rows[j, v:v + V * (Q - 1) + 1:V, :].unsqueeze(0).to_broadcast([G, Q, COLS])
                sp.dma_start(x_lay[v][:, :], src).then_inc(lay_loaded[v], 16)

            def load_hlay(j, u):
                src = h_rows[j, u:u + U * (G - 1) + 1:U, :].unsqueeze(1).to_broadcast([G, Q, COLS])
                sp.dma_start(h_lay[u % NA][:, :], src).then_inc(hlay_loaded[u % NA], 16)

            def store_x(j):
                wait(x_kept, j + 1)
                sp.dma_start(x_rows[j, 0:F, :], x_now[:, :]).then_inc(x_stored, 16)
                sp.dma_start(x_rows[j, F:RING, :], x_now[0:RING - F, :]).then_inc(x_stored, 16)
                wait(x_stored, 32 * j + 32)

            def store_h(j):
                wait(relu0_done, j + 1)
                sp.dma_start(h_rows[j, :, :], r0[0:H, :]).then_inc(h_stored, 16)

            def load_first_hlays(j):
                wait(z_made, at1(j - 1, (U - 1) * V - 1) + 1)
                wait(h_stored, 16 * j + 16)
                load_hlay(j, 0)
                for v in range(V):
                    wait(z_made, at1(j - 1, (U - 1) * V + v) + 1)
                    load_lay(j, v)
                load_hlay(j, 1)

            def load_hlay_after(j, u):
                wait(z_made, at1(j, (u - 1) * V - 1) + 1)
                load_hlay(j, u)

            def body(j, turn):
                load_late_shifts(j)
                store_h(j)
                load_hlay_after(j - 1, 2)
                if turn:
                    store_x(j + 1)
                    load_base(j + 1)
                    load_early_shifts(j + 1)
                load_hlay_after(j - 1, 3)
                load_first_hlays(j)

            sp.dma_start(ids_all[:, :, :], ids.bitcast(U32).rearrange("(t p) f -> p t f", p=P)).then_inc(ids_loaded, 16)
            sp.dma_start(dense_all[:, :, :], dense_ctx.rearrange("(t p) f -> p t f", p=P)).then_inc(dense_loaded, 16)

            sp.wait_ge(w0_zero, 1)
            for a in range(SHIFTS):
                s, k = divmod(a, SH)
                parts = [(0, F - a, F + 1, a, F * a)]
                if a:
                    parts.append((F - a, a, F + 1, (F + 1) * (F - a) + a - F, (F + 1) * (F - a) + F * (a - F)))
                for i0, n, step, row, row_t in parts:
                    p = k * F + i0
                    sp.dma_start(w0[p:p + n, s, :], W0[row:row + step * (n - 1) + 1:step, :]).then_inc(w0_loaded, 16)
                    if a:
                        sp.dma_start(w0t[p:p + n, s, :],
                                     W0[row_t:row_t + step * (n - 1) + 1:step, :]).then_inc(w0_loaded, 16)

            store_x(0)
            load_base(0)
            load_early_shifts(0)
            load_late_shifts(0)
            for v in range(V):
                load_lay(0, v)
            store_h(0)
            sp.wait_ge(h_stored, 16)
            sp.wait_ge(w0_made, 1)
            load_hlay(0, 0)
            load_hlay(0, 1)
            store_x(1)
            load_base(1)
            load_early_shifts(1)

            sp.wait_ge(w1_zero, 1)
            for i in range(F):
                q, v = divmod(i, V)
                sp.dma_start(w1[q:q + Q * (G - 1) + 1:Q, v, :, :],
                             W1[i * H:(i + 1) * H, :].rearrange("(g u) l -> g u l", u=U)).then_inc(w1_loaded, 16)

            sp.wait_ge(wt1_zero, 1)
            sp.dma_start(wt1d[H:P, :], W_top1[0:H, :]).then_inc(top_loaded, 16)
            sp.dma_start(wt1c[:, :], W_top1[H:H + L, :]).then_inc(top_loaded, 16)
            sp.dma_start(wt1d[0:DENSE, :], W_top1[H + L:H + L + DENSE, :]).then_inc(top_loaded, 16)
            sp.dma_start(wt2[:, :, :], W_top2.rearrange("(k p) n -> p k n", p=P)).then_inc(top_loaded, 16)
            sp.dma_start(wt3[:, :], W_top3.rearrange("(k p) o -> p (k o)", p=P)).then_inc(top_loaded, 16)
            sp.dma_start(b1[:, :], b_top1.rearrange("(k p) -> p k", p=P)).then_inc(top_loaded, 16)
            sp.dma_start(b2[:, :], b_top2.rearrange("(k p) -> p k", p=P)).then_inc(top_loaded, 16)

            with sp.Fori(1, TILES - 1) as j:
                body(j, True)
            body(TILES - 1, False)
            for u in range(2, U):
                load_hlay_after(TILES - 1, u)
            sp.wait_ge(y_kept, CH)
            sp.dma_start(y.rearrange("b o -> o b"), y_row[:, :]).then_inc(y_stored, 16)
            sp.wait_ge(y_stored, 16)

        @block.gpsimd
        def _(pool):
            def gather(j):
                if not (isinstance(j, int) and j == 0):
                    pool.wait_ge(x_turned, j)
                nc.gpsimd.tensor_copy(ids_now[:, :], ids_all[:, bass.ds(j, 1), :].rearrange("p t f -> p (t f)")).then_inc(ids_set, 1)
                pool.wait_ge(ids_set, j + 1)
                pool.sem_inc(pool_passed, 1)
                for f in range(F):
                    nc.gpsimd.indirect_dma_start(emb[:, f * D:(f + 1) * D], None, tables[f],
                                                 bass.IndirectOffsetOnAxis(ids_now[:, f:f + 1], 0)).then_inc(gathered, 16)

            nc.gpsimd.memset(w0[:, :, :], 0.0)
            nc.gpsimd.memset(w0t, 0.0).then_inc(w0_zero, 1)
            nc.gpsimd.memset(ident[:, :], 0.0).then_inc(ident_zero, 1)
            pool.wait_ge(ident_zero, 1)
            nc.gpsimd.affine_select(out=ident[:, :], in_=ident[:, :], compare_op=ALU.not_equal, fill=1.0, base=0,
                                    pattern=[[-1, P]], channel_multiplier=1).then_inc(ident_made, 1)
            pool.wait_ge(ids_loaded, 16)
            gather(0)
            nc.gpsimd.memset(w1[:, V - 1, :, :], 0.0).then_inc(w1_zero, 1)
            nc.gpsimd.memset(wt1d[:, :], 0.0).then_inc(wt1_zero, 1)
            nc.gpsimd.memset(feat_d[:, :], 0.0).then_inc(feat_zero, 1)
            with pool.Fori(1, TILES) as j:
                gather(j)

        @block.tensor
        def _(pe):
            def turn_x(j):
                pe.wait_ge(gathered, 16 * F * j + 16 * F)
                if not (isinstance(j, int) and j == 0):
                    pe.wait_ge(relu0_done, j)
                pe.sem_inc(pe_passed, 1)
                e = emb[:, :].rearrange("p (f d) -> p d f", d=D)
                for d in range(D):
                    last = nc.tensor.transpose(psA[0:F, d * P:(d + 1) * P], e[:, d, :], ident[:, :])
                last.then_inc(x_turned, 1)

            def product(ps, place, slot, k, w, first, last):
                pe.wait_ge(z_made, place + 1)
                for c in range(COLS // BANK):
                    cs = slice(c * BANK, (c + 1) * BANK)
                    mm = nc.tensor.matmul(ps[:, cs], w, z[slot][0:k, cs], start=first, stop=last)
                mm.then_inc(z_used, 1)

            def split_product(ps, place, k, w_hi, w_lo, first, last):
                pe.wait_ge(z_lo_made, place + 1)
                for n, (w, zz) in enumerate(((w_hi, z_hi), (w_lo, z_hi), (w_hi, z_lo))):
                    for c in range(COLS // BANK):
                        cs = slice(c * BANK, (c + 1) * BANK)
                        mm = nc.tensor.matmul(ps[:, cs], w, zz[0:k, cs], start=first and n == 0, stop=last and n == 2)
                mm.then_inc(z_used, 1)

            def layer0(j):
                pe.wait_ge(x_kept, j + 1)
                for s in range(STEPS0):
                    k = step_rows(s)
                    if s in SPLIT0:
                        n = SPLIT0.index(s)
                        split_product(psA, split0(j, s), k, w0_hi[0:k, n, :], w0_lo[0:k, n, :], s == 0, s == STEPS0 - 1)
                    else:
                        product(psA, at0(j, s), slot0(j, s), k, w0[0:k, s, :], s == 0, s == STEPS0 - 1)

            def layer1(j, steps):
                for s in steps:
                    u, v = divmod(s, V)
                    if s in SPLIT1:
                        n = SPLIT1.index(s)
                        split_product(psB, split1(j, s), P, w1_hi[:, n, :], w1_lo[:, n, :], s == 0, s == STEPS1 - 1)
                    else:
                        product(psB, at1(j, s), slot1(j, s), P, w1[:, v, u, :], s == 0, s == STEPS1 - 1)

            def body(j, turn):
                layer0(j)
                if not (isinstance(j, int) and j == 1):
                    pe.wait_ge(relu1_done, j - 1)
                layer1(j - 1, range(0, 4))
                if turn:
                    turn_x(j + 1)
                layer1(j - 1, range(4, STEPS1))

            pe.wait_ge(ident_made, 1)
            pe.wait_ge(dense_loaded, 16)
            for t in range(TILES):
                last = nc.tensor.transpose(psB[0:DENSE, t * P:(t + 1) * P], dense_all[:, t, :], ident[:, :])
            last.then_inc(dense_turned, 1)
            turn_x(0)
            pe.wait_ge(w0_made, 1)
            pe.wait_ge(w_split, len(SPLIT0))
            layer0(0)
            turn_x(1)
            pe.wait_ge(w1_loaded, 16 * F)
            pe.wait_ge(w_split, SPLITS)
            pe.wait_ge(dense_kept, 1)
            body(1, True)
            with pe.Fori(2, TILES - 1) as j:
                body(j, True)
            body(TILES - 1, False)
            pe.wait_ge(relu1_done, TILES - 1)
            layer1(TILES - 1, range(STEPS1))

            def top1(c):
                cs = slice(c * BANK, (c + 1) * BANK)
                for m in range(K1):
                    if c:
                        pe.wait_ge(top1_kept, (c - 1) * K1 + m + 1)
                    nc.tensor.matmul(psA[:, m * BANK:(m + 1) * BANK], wt1c[:, m * P:(m + 1) * P], feat_c[:, cs],
                                     start=True, stop=False)
                    nc.tensor.matmul(psA[:, m * BANK:(m + 1) * BANK], wt1d[:, m * P:(m + 1) * P], feat_d[:, cs],
                                     start=False, stop=True).then_inc(top1_done, 1)

            pe.wait_ge(top_loaded, 16 * 7)
            pe.wait_ge(feat_zero, 1)
            pe.wait_ge(sum0_done, TILES)
            pe.wait_ge(sum1_done, TILES)
            top1(0)
            for c in range(CH):
                if c + 1 < CH:
                    top1(c + 1)
                for m in range(K2):
                    if c:
                        pe.wait_ge(top2_kept, (c - 1) * K2 + m + 1)
                    for k in range(K1):
                        pe.wait_ge(top1_kept, c * K1 + k + 1)
                        mm = nc.tensor.matmul(psB[:, m * BANK:(m + 1) * BANK], wt2[:, k, m * P:(m + 1) * P],
                                              hid1[c % 2][:, k, :], start=(k == 0), stop=(k == K1 - 1))
                    mm.then_inc(top2_done, 1)
                if c:
                    pe.wait_ge(y_kept, c)
                for k in range(K2):
                    pe.wait_ge(top2_kept, c * K2 + k + 1)
                    mm = nc.tensor.matmul(psB[0:1, K2 * BANK:(K2 + 1) * BANK], wt3[:, k:k + 1], hid2[c % 2][:, k, :],
                                          start=(k == 0), stop=(k == K2 - 1))
                mm.then_inc(top3_done, 1)

        @block.scalar
        def _(act):
            def keep_x(j):
                act.wait_ge(x_turned, j + 1)
                if not (isinstance(j, int) and j < 3):
                    act.wait_ge(sum1_done, j - 2)
                if isinstance(j, int) and j == 1:
                    act.wait_ge(x_stored, 32)
                nc.scalar.activation(x_now, psA[0:F, :], ACT.Copy).then_inc(x_kept, 1)

            def relu0(j):
                act.wait_ge(z_used, at0(j, STEPS0 - 1) + 1)
                if not (isinstance(j, int) and j == 0):
                    act.wait_ge(h_stored, 16 * j)
                    act.wait_ge(sum0_done, j)
                nc.scalar.activation(r0[:, :], psA[:, :], ACT.Relu).then_inc(relu0_done, 1)

            def relu1(j, x_tiles):
                act.wait_ge(z_used, at1(j, STEPS1 - 1) + 1)
                act.wait_ge(x_stored, 32 * x_tiles)
                if not (isinstance(j, int) and j == 0):
                    act.wait_ge(sum1_done, j)
                nc.scalar.activation(r1[:, :], psB[:, :], ACT.Relu).then_inc(relu1_done, 1)

            def high(place, k, prior):
                act.wait_ge(z_made, place + 1)
                if prior is not None:
                    act.wait_ge(z_used, prior + 1)
                nc.scalar.activation(z_hi[0:k, :], z_split[0:k, :], ACT.Copy).then_inc(z_hi_made, 1)

            def high0(j, s):
                n = SPLIT0.index(s)
                if n:
                    prior = at0(j, SPLIT0[n - 1])
                elif isinstance(j, int) and j < 2:
                    prior = at0(0, SPLIT0[-1]) if j else None
                else:
                    prior = at1(j - 2, SPLIT1[-1])
                high(at0(j, s), step_rows(s), prior)

            def high1(j, s):
                n = SPLIT1.index(s)
                if n:
                    prior = at1(j, SPLIT1[n - 1])
                elif isinstance(j, int) and j == TILES - 1:
                    prior = at1(j - 1, SPLIT1[-1])
                else:
                    prior = at0(j + 1, SPLIT0[-1])
                high(at1(j, s), P, prior)

            def body(j, turn):
                high0(j, SPLIT0[0])
                if not (isinstance(j, int) and j == 1):
                    relu1(j - 2, j + 1)
                for s in SPLIT0[1:]:
                    high0(j, s)
                for s in SPLIT1:
                    high1(j - 1, s)
                    if s == 0:
                        relu0(j)
                    if turn and s == 6:
                        keep_x(j + 1)

            act.wait_ge(dense_turned, 1)
            act.wait_ge(feat_zero, 1)
            nc.scalar.activation(feat_d[0:DENSE, :], psB[0:DENSE, :], ACT.Copy).then_inc(dense_kept, 1)
            act.wait_ge(w0_made, 1)
            for n, s in enumerate(SPLIT0):
                nc.scalar.activation(w0_hi[:, n, :], w0[:, s, :], ACT.Copy).then_inc(w_hi_made, 1)
            keep_x(0)
            for s in SPLIT0:
                high0(0, s)
            relu0(0)
            keep_x(1)
            act.wait_ge(w1_loaded, 16 * F)
            for n, s in enumerate(SPLIT1):
                u, v = divmod(s, V)
                nc.scalar.activation(w1_hi[:, n, :], w1[:, v, u, :], ACT.Copy).then_inc(w_hi_made, 1)
            body(1, True)
            with act.Fori(2, TILES - 1) as j:
                body(j, True)
            body(TILES - 1, False)
            last = TILES - 1
            for s in SPLIT1:
                high1(last, s)
                if s == 0:
                    relu1(last - 1, TILES)
            relu1(last, TILES)

            act.wait_ge(top_loaded, 16 * 7)
            act.wait_ge(z_made, TILES * STEPS)

            def top1_keep(c):
                for m in range(K1):
                    act.wait_ge(top1_done, c * K1 + m + 1)
                    if c >= 2:
                        act.wait_ge(top2_done, (c - 1) * K2)
                    nc.scalar.activation(hid1[c % 2][:, m, :], psA[:, m * BANK:(m + 1) * BANK], ACT.Relu,
                                         bias=b1[:, m:m + 1]).then_inc(top1_kept, 1)

            top1_keep(0)
            for c in range(CH):
                if c + 1 < CH:
                    top1_keep(c + 1)
                for m in range(K2):
                    act.wait_ge(top2_done, c * K2 + m + 1)
                    if c >= 2:
                        act.wait_ge(top3_done, c - 1)
                    nc.scalar.activation(hid2[c % 2][:, m, :], psB[:, m * BANK:(m + 1) * BANK], ACT.Relu,
                                         bias=b2[:, m:m + 1]).then_inc(top2_kept, 1)
                act.wait_ge(top3_done, c + 1)
                nc.scalar.activation(y_row[:, c * BANK:(c + 1) * BANK], psB[0:1, K2 * BANK:(K2 + 1) * BANK],
                                     ACT.Copy).then_inc(y_kept, 1)

        @block.vector
        def _(dve):
            def make(z_out, k, a, b):
                nc.vector.tensor_tensor(z_out[0:k, :], a[0:k, :], b[0:k, :], ALU.mult).then_inc(z_made, 1)

            def low(k, place):
                dve.wait_ge(z_hi_made, place + 1)
                nc.vector.tensor_tensor(z_lo[0:k, :], z_split[0:k, :], z_hi[0:k, :].bitcast(FP),
                                        ALU.subtract).then_inc(z_lo_made, 1)

            def layer0(j, steps):
                for s in steps:
                    if s == 0:
                        dve.wait_ge(base_loaded, 48 * j + 48)
                        dve.wait_ge(first_loaded, 48 * j + 48)
                        other = x_first
                    else:
                        n = (s - 1) % NX
                        loads = [step_rows(t) // F if t <= s else 0 for t in range(n + 1, STEPS0, NX)]
                        a_tile = sum(step_rows(t) // F for t in range(n + 1, STEPS0, NX))
                        dve.wait_ge(shift_loaded[n], 16 * a_tile * j + 16 * sum(loads))
                        other = x_shift[n]
                    if s in SPLIT0:
                        if not (isinstance(j, int) and j == 0 and s == SPLIT0[0]):
                            dve.wait_ge(z_lo_made, split0(j, s))
                        make(z_split, step_rows(s), x_base, other)
                    else:
                        if before0(j, s) is not None:
                            dve.wait_ge(z_used, before0(j, s) + 1)
                        make(z[slot0(j, s)], step_rows(s), x_base, other)
                    if s - 1 in SPLIT0:
                        low(step_rows(s - 1), split0(j, s - 1))

            def layer1(j, steps):
                for s in steps:
                    u, v = divmod(s, V)
                    if v == 0:
                        dve.wait_ge(hlay_loaded[u % NA], 32 * j + 16 * (u // NA) + 16)
                    if u == 0:
                        dve.wait_ge(lay_loaded[v], 16 * j + 16)
                    if s in SPLIT1:
                        dve.wait_ge(z_lo_made, split1(j, s))
                        make(z_split, P, h_lay[u % NA], x_lay[v])
                    else:
                        dve.wait_ge(z_used, before1(j, s) + 1)
                        make(z[slot1(j, s)], P, h_lay[u % NA], x_lay[v])
                    if s - 1 in SPLIT1:
                        low(P, split1(j, s - 1))

            def sum_over_d(r, rows, n, out, done):
                width = COLS // 2
                for step in range(3):
                    nc.vector.tensor_tensor(r[rows, 0:width], r[rows, 0:width], r[rows, width:2 * width],
                                            ALU.add).then_inc(sum_step, 1)
                    dve.wait_ge(sum_step, 3 * n + step + 1)
                    width //= 2
                nc.vector.tensor_tensor(out, r[rows, 0:width], r[rows, width:2 * width], ALU.add).then_inc(done, 1)

            def sum0(j, n):
                dve.wait_ge(relu0_done, j + 1)
                sum_over_d(r0, slice(H, P), n, feat_d[H:P, bass.ds(j * P, P)], sum0_done)

            def sum1(j, n):
                dve.wait_ge(relu1_done, j + 1)
                sum_over_d(r1, slice(0, P), n, feat_c[:, bass.ds(j * P, P)], sum1_done)

            def body(j):
                layer0(j, range(0, 6))
                if not (isinstance(j, int) and j == 1):
                    sum1(j - 2, 2 * j - 2)
                layer0(j, range(6, STEPS0))
                layer1(j - 1, range(0, 6))
                sum0(j, 2 * j - 1)
                layer1(j - 1, range(6, STEPS1))

            dve.wait_ge(w0_loaded, 16 * (4 * SHIFTS - 3))
            nc.vector.tensor_tensor(w0[:, :, :], w0[:, :, :], w0t, ALU.add).then_inc(w0_made, 1)
            for n, s in enumerate(SPLIT0):
                dve.wait_ge(w_hi_made, n + 1)
                nc.vector.tensor_tensor(w0_lo[:, n, :], w0[:, s, :], w0_hi[:, n, :].bitcast(FP),
                                        ALU.subtract).then_inc(w_split, 1)
            dve.wait_ge(feat_zero, 1)
            layer0(0, range(STEPS0))
            sum0(0, 0)
            for n, s in enumerate(SPLIT1):
                u, v = divmod(s, V)
                dve.wait_ge(w_hi_made, len(SPLIT0) + n + 1)
                nc.vector.tensor_tensor(w1_lo[:, n, :], w1[:, v, u, :], w1_hi[:, n, :].bitcast(FP),
                                        ALU.subtract).then_inc(w_split, 1)
            body(1)
            with dve.Fori(2, TILES) as j:
                body(j)
            last = TILES - 1
            layer1(last, range(0, 6))
            sum1(last - 1, 2 * last)
            layer1(last, range(6, STEPS1))
            sum1(last, 2 * last + 1)


def kernel(**inputs):
    import numpy as np
    import concourse.bacc as bacc
    from concourse.bass_utils import run_bass_kernel_spmd

    nc = bacc.Bacc("TRN2", target_bir_lowering=False, num_devices=1)
    arrays = {}

    def given(name):
        a = np.ascontiguousarray(inputs[name])
        arrays[f"in_{name}"] = a
        return nc.dram_tensor(f"in_{name}", a.shape, mybir.dt.from_np(a.dtype), kind="ExternalInput").ap()

    y = nc.dram_tensor("out_y", (B, 1), FP, kind="ExternalOutput").ap()
    tower(nc, given("dense_ctx"), given("ids"), [given(f"tbl_{f}") for f in range(F)], given("W_top1"),
          given("b_top1"), given("W_top2"), given("b_top2"), given("W_top3"), given("L0_rec_W0"),
          given("L0_rec_W1"), y)
    r = run_bass_kernel_spmd(nc, [arrays], core_ids=[0])
    return r.results[0]["out_y"]
```
